# Optimizing a Trainium2 kernel written in Bass

```python
import numpy as np
import jax
import jax.numpy as jnp

def _softmax(x, axis=-1):
    return jax.nn.softmax(x, axis=axis)

def _gelu(x):
    return jax.nn.gelu(x, approximate=True)

def _silu(x):
    return jax.nn.silu(x)

def _sigmoid(x):
    return jax.nn.sigmoid(x)

def _layernorm(x, axis=-1, eps=1e-05):
    m = jnp.mean(x, axis=axis, keepdims=True)
    v = jnp.var(x, axis=axis, keepdims=True)
    return (x - m) / jnp.sqrt(v + eps)

def _scatter_add(tgt, idx, src, axis=0):
    return tgt.at[idx].add(src)

def _segment_sum(src, seg, n):
    return jax.ops.segment_sum(src, seg, n)
kernel_name = 'mk_rec_standalone_d1_rec_r8_981db7'

def setup_inputs(seed: int=0):
    np.random.seed(seed)
    _w = jnp.asarray

    def _rec_inputs():
        import jax
        import jax.numpy as jnp
        _rk = jax.random.key(seed)
        r_query = -9.80646e-05 + 1.00041 * jax.random.normal(jax.random.fold_in(_rk, 1), (2048, 128), jnp.float32)
        r_keys = -9.97791e-05 + 0.999858 * jax.random.normal(jax.random.fold_in(_rk, 2), (2048, 200, 128), jnp.float32)
        r_mask = jax.random.randint(jax.random.fold_in(_rk, 3), (2048, 200), 0, 2, jnp.int32)
        return (r_query, r_keys, r_mask)
    r_query, r_keys, r_mask = _rec_inputs()

    def _L0_rec_setup():
        import jax, jax.numpy as jnp
        import numpy as np
        EMBED_DIM = 128
        HIDDEN_DIM = 64
        BATCH = 512
        SEQ_LEN = 200
        NEG_INF = -1000000000.0
        key = jax.random.key(seed)
        ks = jax.random.split(key, 9)
        d, h = (EMBED_DIM, HIDDEN_DIM)
        query = jax.random.normal(ks[0], (BATCH, d), dtype=jnp.float32)
        keys = jax.random.normal(ks[1], (BATCH, SEQ_LEN, d), dtype=jnp.float32)
        mask = jax.random.randint(ks[2], (BATCH, SEQ_LEN), 0, 2, dtype=jnp.int32)
        s1 = 1.0 / np.sqrt(4 * d)
        s2 = 1.0 / np.sqrt(h)
        W1 = jax.random.uniform(ks[3], (4 * d, h), jnp.float32, -s1, s1)
        b1 = jax.random.uniform(ks[4], (h,), jnp.float32, -s1, s1)
        W2 = jax.random.uniform(ks[5], (h, h), jnp.float32, -s2, s2)
        b2 = jax.random.uniform(ks[6], (h,), jnp.float32, -s2, s2)
        W3 = jax.random.uniform(ks[7], (h, 1), jnp.float32, -s2, s2)
        b3 = jax.random.uniform(ks[8], (1,), jnp.float32, -s2, s2)
        return {'query': query, 'keys': keys, 'mask': mask, 'W1': W1, 'b1': b1, 'W2': W2, 'b2': b2, 'W3': W3, 'b3': b3}
    _L0_rec_all = _L0_rec_setup()
    _L0_rec_in = {k: v for k, v in _L0_rec_all.items() if k in ('W1', 'b1', 'W2', 'b2', 'W3', 'b3')}
    del _L0_rec_all
    return {'r_query': r_query, 'r_keys': r_keys, 'r_mask': r_mask, 'L0_rec_W1': _L0_rec_in['W1'], 'L0_rec_b1': _L0_rec_in['b1'], 'L0_rec_W2': _L0_rec_in['W2'], 'L0_rec_b2': _L0_rec_in['b2'], 'L0_rec_W3': _L0_rec_in['W3'], 'L0_rec_b3': _L0_rec_in['b3']}

def reference(r_query, r_keys, r_mask, L0_rec_W1, L0_rec_b1, L0_rec_W2, L0_rec_b2, L0_rec_W3, L0_rec_b3):
    import jax
    import jax.numpy as jnp

    def _L0_rec_ref(query, keys, mask, W1, b1, W2, b2, W3, b3):
        import jax, jax.numpy as jnp
        import numpy as np
        EMBED_DIM = 128
        HIDDEN_DIM = 64
        BATCH = 512
        SEQ_LEN = 200
        NEG_INF = -1000000000.0
        q = jnp.broadcast_to(query[:, None, :], keys.shape)
        att_input = jnp.concatenate([q, keys, q - keys, q * keys], axis=-1)
        h1 = jax.nn.relu(jnp.einsum('bsk,kh->bsh', att_input, W1) + b1)
        h2 = jax.nn.relu(jnp.einsum('bsh,hg->bsg', h1, W2) + b2)
        scores = (jnp.einsum('bsg,go->bso', h2, W3) + b3)[..., 0]
        scores = jnp.where(mask == 0, NEG_INF, scores)
        weights = jax.nn.softmax(scores, axis=-1)
        output = jnp.einsum('bs,bsd->bd', weights, keys)
        return output
    y = _L0_rec_ref(r_query, r_keys, r_mask, L0_rec_W1, L0_rec_b1, L0_rec_W2, L0_rec_b2, L0_rec_W3, L0_rec_b3)
    return y

_drawn_inputs = setup_inputs


def setup_inputs(seed=0):
    import zlib

    import numpy as np

    out = dict(_drawn_inputs(seed))
    spreads = {}
    factors = {'L0_rec_b1': 8.0, 'L0_rec_b2': 2.989}
    for name, (base, spread) in spreads.items():
        noise = np.random.default_rng([zlib.crc32(name.encode()), seed]).standard_normal(out[name].shape)
        drawn = base * np.exp(spread * noise) if base else spread * noise
        out[name] = jnp.asarray(drawn.astype(out[name].dtype))
    for name, factor in factors.items():
        out[name] = (out[name] * factor).astype(out[name].dtype)
    return out
```

```python
from contextlib import ExitStack

import concourse.bass as bass
from concourse import mybir
from concourse.alu_op_type import AluOpType as ALU

F32 = mybir.dt.float32
I32 = mybir.dt.int32
U8 = mybir.dt.uint8
ACT = mybir.ActivationFunctionType
AX = mybir.AxisListType

P = 128
NEG_INF = -1000000000.0


def din_attention(nc, query, keys, mask, w1, b1, w2, b2, w3, b3, out):
    B, S, D = keys.shape
    H = w2.shape[0]
    CB = 16
    TOK = CB * S
    J = TOK // P
    R = P // CB
    NCH = B // CB
    GC = 2
    NG = NCH // GC
    RING = 8
    GI = RING // GC
    ITERS = NCH // RING
    Q = 4
    QR = CB // Q
    PAIRS = QR // 2
    QT = QR * S // 2
    TSPLIT = [4, 4, 4, 4, 3, 3, 3]
    NT = len(TSPLIT)
    TSTART = [sum(TSPLIT[:t]) for t in range(NT)]
    LAST = NCH + 5
    assert D == P and R * J == S and sum(TSPLIT) == J and 2 * H == P

    keys_c = keys.rearrange("(n i) s d -> n (i s d)", i=CB).rearrange("n (p f) -> n p f", p=P)
    mask_g = mask.rearrange("(h g c q v) s -> h q c v g s", h=2, c=GC, q=Q, v=QR)
    out_g = out.rearrange("(g c i) d -> g c i d", c=GC, i=CB)

    with ExitStack() as ctx:
        def sb(name, shape, dt=F32):
            return ctx.enter_context(nc.sbuf_tensor(name, shape, dt))

        def ps(name):
            return ctx.enter_context(nc.psum_tensor(name, [P, 512], F32))

        def sem(name):
            return ctx.enter_context(nc.semaphore(name))

        ring = sb("ring", [P, RING, J * D])
        kt = sb("kt", [P, 2, J, P])
        we = sb("we", [P, 2, CB, H])
        h1 = sb("h1", [P, 2, QT])
        h2 = sb("h2", [P, 2, CB // 2, S])
        qt = sb("qt", [P, B])
        bias1 = sb("bias1", [P, B // 2])
        w1_sb = sb("w1_sb", [P, 4, H])
        w_key = sb("w_key", [P, H])
        w_query = sb("w_query", [P, H])
        w2_sb = sb("w2_sb", [P, P])
        w3_col = sb("w3_col", [P, 1])
        w3_sb = sb("w3_sb", [P, GC * PAIRS, 32])
        b1_sb = sb("b1_sb", [P, 1])
        b2_sb = sb("b2_sb", [P, 1])
        b3_sb = sb("b3_sb", [P, 1])
        ident = sb("ident", [P, P])
        own = sb("own", [P, CB])
        dropped = sb("dropped", [P, NG, S], U8)
        drop = sb("drop", [P, 2, S], U8)
        neg = sb("neg", [P, S])
        sc = sb("sc", [P, 2, S])
        pr = sb("pr", [P, 2, S])
        nmax = sb("nmax", [P, 2])
        rsum = sb("rsum", [P, 2])
        rinv = sb("rinv", [P, 2])
        pn = sb("pn", [P, 2, GC, J])
        pw = sb("pw", [P, 2, GC, J, CB])
        oh = sb("oh", [P, D])
        osb = sb("osb", [P, 2, D])
        q_nat = h2[:, :, :, :].rearrange("p a b s -> p (a b s)")[:, 0:B // P * D].rearrange(
            "p (n d) -> p n d", d=D)
        mstage = ring[:, RING - 4:RING, :].rearrange("p a f -> p (a f)").bitcast(I32)[:, :].rearrange(
            "p (g s) -> p g s", s=S)

        ps_t = [ps("ps_t0"), ps("ps_t1")]
        ps_1 = [ps("ps_10"), ps("ps_11")]
        ps_2 = [ps("ps_20"), ps("ps_21")]
        ps_s = ps("ps_s")
        ps_o = ps("ps_o")

        query_loaded = sem("query_loaded")
        weights_loaded = sem("weights_loaded")
        stage_cleared = sem("stage_cleared")
        mask_loaded = sem("mask_loaded")
        mask_done = sem("mask_done")
        keys_loaded = [sem(f"keys_loaded{i}") for i in range(RING)]
        ident_ready = sem("ident_ready")
        consts = sem("consts")
        pool_chain = sem("pool_chain")
        w1_ready = sem("w1_ready")
        q_transposed = sem("q_transposed")
        q_copied = sem("q_copied")
        qw_done = sem("qw_done")
        bias1_ready = sem("bias1_ready")
        t_done = sem("t_done")
        kt_copied = sem("kt_copied")
        we_ready = sem("we_ready")
        we_mult = sem("we_mult")
        drop_ready = sem("drop_ready")
        l1_done = sem("l1_done")
        relu1_done = sem("relu1_done")
        l2_done = sem("l2_done")
        relu2_done = sem("relu2_done")
        l3_done = sem("l3_done")
        scores_copied = sem("scores_copied")
        masked = sem("masked")
        max_ready = sem("max_ready")
        exp_done = sem("exp_done")
        rinv_ready = sem("rinv_ready")
        probs_ready = sem("probs_ready")
        spread = [sem(f"spread{i}") for i in range(2)]
        pw_ready = sem("pw_ready")
        out_done = sem("out_done")
        half_copied = sem("half_copied")
        out_ready = sem("out_ready")
        stored = [sem(f"stored{i}") for i in range(2)]

        def wait(eng, s, it, per, const):
            v = it * per + const
            if not isinstance(v, int) or v > 0:
                eng.wait_ge(s, v)

        def steps(eng, body):
            for sl in range(RING):
                body(0, sl)
            with eng.Fori(1, ITERS) as it:
                for sl in range(RING):
                    body(it, sl)
            for sl in range(LAST - NCH):
                body(ITERS, sl)

        def real(it, off, n, per):
            return not isinstance(it, int) or 0 <= it * per + off < n

        block = ctx.enter_context(nc.Block())

        @block.sync
        def _(sp):
            sp.dma_start(q_nat, query.rearrange("(n p) d -> p n d", p=P)).then_inc(query_loaded, 16)
            sp.dma_start(w1_sb[:, :, :], w1.rearrange("(b d) h -> d b h", d=D)).then_inc(query_loaded, 16)

            def index(v):
                return v if isinstance(v, int) else sp.snap(v)

            def load(n, sl):
                sp.dma_start(ring[:, sl, :], keys_c[n]).then_inc(keys_loaded[sl], 16)

            for sl in range(RING - 4):
                load(sl, sl)
            sp.wait_ge(stage_cleared, 1)
            for half in range(2):
                for q in range(Q):
                    for c in range(GC):
                        p0 = 32 * q + QR * c
                        sp.dma_start(mstage[p0:p0 + QR, half * NG // 2:(half + 1) * NG // 2, :],
                                     mask_g[half, q, c]).then_inc(mask_loaded, 16)
            sp.wait_ge(mask_done, 1)
            for sl in range(RING - 4, RING):
                load(sl, sl)

            def store(it, gl):
                par = gl % 2
                g = index(it * GI + gl)
                wait(sp, out_ready, it, GI, gl + 1)
                for c in range(GC):
                    sp.dma_start(out_g[g, c], osb[32 * c:32 * c + CB, par, :]).then_inc(stored[par], 16)

            def group(it, gl, load_next, store_last):
                par = gl % 2
                wait(sp, probs_ready, it, GI, gl + 1)
                if not load_next:
                    wait(sp, pw_ready, it, GI, gl - 1)
                for q in range(Q):
                    for c in range(GC):
                        p0 = 32 * q + QR * c
                        sp.dma_start(pn[32 * q:32 * q + 32, par, c, :],
                                     pr[p0:p0 + QR, par, :].rearrange("v (r j) -> v r j", j=J)
                                     ).then_inc(spread[par], 16)
                if store_last:
                    store(it, gl - 1)
                if load_next:
                    n = [index((it + 1) * RING + GC * gl + c) for c in range(GC)]
                    wait(sp, out_done, it, GI, gl + 1)
                    for c in range(GC):
                        load(n[c], GC * gl + c)

            for gl in range(GI):
                group(0, gl, True, gl > 0)
            with sp.Fori(1, ITERS - 1) as it:
                for gl in range(GI):
                    group(it, gl, True, True)
            for gl in range(GI):
                group(ITERS - 1, gl, False, True)
            store(ITERS - 1, GI - 1)
            for par in range(2):
                sp.wait_ge(stored[par], 16 * GC * NG // 2)

        @block.gpsimd
        def _(pool):
            nc.gpsimd.memset(ident[:, :], 0.0).then_inc(pool_chain, 1)
            nc.gpsimd.memset(own[:, :], 1.0).then_inc(pool_chain, 1)
            pool.wait_ge(pool_chain, 2)
            nc.gpsimd.affine_select(out=ident[:, :], in_=ident[:, :], compare_op=ALU.not_equal, fill=1.0,
                                    base=0, pattern=[[-1, P]], channel_multiplier=1).then_inc(ident_ready, 1)
            nc.gpsimd.affine_select(out=own[:, :], in_=own[:, :], compare_op=ALU.is_ge, fill=0.0,
                                    base=0, pattern=[[-R, CB]], channel_multiplier=1).then_inc(pool_chain, 1)
            pool.wait_ge(pool_chain, 3)
            nc.gpsimd.affine_select(out=own[:, :], in_=own[:, :], compare_op=ALU.is_ge, fill=0.0,
                                    base=R - 1, pattern=[[R, CB]], channel_multiplier=-1).then_inc(pool_chain, 1)
            pool.wait_ge(pool_chain, 4)
            pool.wait_ge(w1_ready, 2)
            pool.wait_ge(q_copied, 4)

            def weights(it, off):
                par = off % 2
                if isinstance(it, int):
                    qc = qt[:, (it * RING + off) * CB:(it * RING + off + 1) * CB]
                else:
                    qc = qt[:, bass.ds(it * (RING * CB) + off * CB, CB)]
                wait(pool, l1_done, it, RING * Q, Q * (off - 1))
                nc.gpsimd.tensor_tensor(we[:, par], w1_sb[:, 3:4, :].to_broadcast([P, CB, H]),
                                        qc.unsqueeze(2).to_broadcast([P, CB, H]), ALU.mult).then_inc(we_mult, 1)
                wait(pool, we_mult, it, RING, off + 1)
                nc.gpsimd.tensor_tensor(we[:, par], we[:, par], w_key[:, :].unsqueeze(1).to_broadcast([P, CB, H]),
                                        ALU.add).then_inc(we_ready, 1)

            def spread_probs(it, gl, par):
                wait(pool, spread[par], it, GI // 2 * 16 * Q * GC, (gl // 2 + 1) * 16 * Q * GC)
                wait(pool, out_done, it, GI, gl - 1)
                for c in range(GC):
                    ins = nc.gpsimd.tensor_tensor(pw[:, par, c], pn[:, par, c, :].unsqueeze(2).to_broadcast([P, J, CB]),
                                                  own[:, :].unsqueeze(1).to_broadcast([P, J, CB]), ALU.mult)
                ins.then_inc(pw_ready, 1)

            def take_mask(it, gl):
                if isinstance(it, int):
                    part = dropped[:, it * GI + gl, :]
                else:
                    part = dropped[:, bass.ds(it * GI + gl, 1), :].rearrange("p a s -> p (a s)")
                if isinstance(it, int) and it == 0 and gl == 0:
                    pool.wait_ge(mask_done, 1)
                wait(pool, masked, it, GI, gl - 1)
                nc.gpsimd.tensor_copy(drop[:, gl % 2, :], part).then_inc(drop_ready, 1)

            def body(it, sl):
                if real(it, sl, NCH, RING):
                    weights(it, sl)
                    if sl % GC == 1:
                        take_mask(it, sl // GC)
                gl = (sl - 4) // GC
                if sl % GC == 0 and real(it, gl, NG, GI):
                    spread_probs(it, gl, gl % 2)

            steps(pool, body)

        @block.scalar
        def _(act):
            act.dma_start(w2_sb[0:H, 0:H], w2).then_inc(weights_loaded, 16)
            act.dma_start(w2_sb[H:P, H:P], w2).then_inc(weights_loaded, 16)
            for half in range(2):
                p0 = half * H
                act.dma_start(w3_col[p0:p0 + H, :], w3).then_inc(weights_loaded, 16)
                act.dma_start(b1_sb[p0:p0 + H, :], b1.rearrange("(h a) -> h a", a=1)).then_inc(weights_loaded, 16)
                act.dma_start(b2_sb[p0:p0 + H, :], b2.rearrange("(h a) -> h a", a=1)).then_inc(weights_loaded, 16)
            act.dma_start(b3_sb[:, :], b3.rearrange("(h a) -> h a", a=1).to_broadcast([P, 1])).then_inc(weights_loaded, 16)
            act.wait_ge(weights_loaded, 16 * 9)
            for n in range(B // 2 // 512):
                act.wait_ge(qw_done, n + 1)
                nc.scalar.activation(bias1[:, 512 * n:512 * (n + 1)], ps_1[n % 2][:, :], ACT.Identity,
                                     bias=b1_sb[:, :]).then_inc(bias1_ready, 1)
            act.wait_ge(bias1_ready, B // 2 // 512)

            def relu1(it, off, qd):
                m = Q * off + qd
                wait(act, l1_done, it, RING * Q, m + 1)
                wait(act, l2_done, it, RING * Q, m - 1)
                for u in range(PAIRS):
                    if isinstance(it, int):
                        pair = (it * RING * Q + m) * PAIRS + u
                        bias = bias1[:, pair:pair + 1]
                    else:
                        bias = bias1[:, bass.ds(it * (RING * Q * PAIRS) + m * PAIRS + u, 1)]
                    ins = nc.scalar.activation(h1[:, m % 2, u * S:(u + 1) * S], ps_1[m % 2][:, u * S:(u + 1) * S],
                                               ACT.Relu, bias=bias)
                ins.then_inc(relu1_done, 1)

            def relu2(it, m):
                wait(act, l2_done, it, RING * Q, m + 1)
                off = m // Q
                if m % Q == 0:
                    wait(act, l3_done, it, RING, off - 1)
                nc.scalar.activation(h2[:, off % 2, PAIRS * (m % Q):PAIRS * (m % Q + 1), :],
                                     ps_2[m % 2][:, 0:QT].rearrange("p (u s) -> p u s", s=S),
                                     ACT.Relu, bias=b2_sb[:, :]).then_inc(relu2_done, 1)

            def copy_scores(it, gl):
                wait(act, l3_done, it, RING, GC * (gl + 1))
                wait(act, exp_done, it, GI, gl - 1)
                nc.scalar.activation(sc[:, gl % 2, :].rearrange("p (r j) -> p r j", j=J),
                                     ps_s[:, 0:S].rearrange("p (j r) -> p r j", r=R),
                                     ACT.Identity, bias=b3_sb[:, :]).then_inc(scores_copied, 1)

            def exps(it, gl):
                par = gl % 2
                wait(act, max_ready, it, GI, gl + 1)
                wait(act, spread[par], it, GI // 2 * 16 * Q * GC, (gl // 2) * 16 * Q * GC)
                nc.scalar.activation(pr[:, par, :], sc[:, par, :], ACT.Exp, bias=nmax[:, par:par + 1],
                                     accum_out=rsum[:, par:par + 1]).then_inc(exp_done, 1)

            def copy_half(it, gl):
                wait(act, out_done, it, GI, gl + 1)
                wait(act, out_ready, it, GI, gl)
                nc.scalar.activation(oh[0:32 + CB, :], ps_o[64:96 + CB, 0:D], ACT.Copy).then_inc(half_copied, 1)

            def body(it, sl):
                for qd in range(Q):
                    if real(it, sl - 1, NCH, RING):
                        relu1(it, sl - 1, qd)
                    m = Q * (sl - 1) + qd - 1
                    if real(it, m, NCH * Q, RING * Q):
                        relu2(it, m)
                    gl = (sl - 3) // GC
                    if sl % GC == 1 and real(it, gl, NG, GI):
                        if qd == 1:
                            copy_scores(it, gl)
                        if qd == 2:
                            exps(it, gl)
                    gl = (sl - 6) // GC
                    if sl % GC == 0 and qd == 0 and real(it, gl, NG, GI):
                        copy_half(it, gl)

            steps(act, body)

        @block.tensor
        def _(pe):
            pe.wait_ge(ident_ready, 1)
            pe.wait_ge(query_loaded, 32)
            for n in range(B // P // 4):
                if n >= 2:
                    pe.wait_ge(q_copied, n - 1)
                for t in range(4):
                    mm = pe.transpose(ps_t[n % 2][:, t * P:(t + 1) * P], q_nat[:, 4 * n + t, :], ident[:, :])
                mm.then_inc(q_transposed, 1)
            pe.wait_ge(w1_ready, 2)
            pe.wait_ge(q_copied, B // P // 4)
            for n in range(B // 2 // 512):
                for half in range(2):
                    mm = pe.matmul(ps_1[n % 2][half * H:(half + 1) * H, :], w_query[:, :],
                                   qt[:, 1024 * n + half:1024 * (n + 1):2], start=True, stop=True)
                mm.then_inc(qw_done, 1)
            pe.wait_ge(bias1_ready, B // 2 // 512)
            pe.wait_ge(weights_loaded, 16 * 9)
            pe.wait_ge(consts, 3)

            def transposes(it, sl, t):
                n = NT * sl + t
                if t == 0:
                    pe.wait_ge(keys_loaded[sl], (it + 1) * 16)
                wait(pe, kt_copied, it, RING * NT, n - 1)
                for a in range(TSPLIT[t]):
                    j = TSTART[t] + a
                    mm = pe.transpose(ps_t[n % 2][:, a * P:(a + 1) * P], ring[:, sl, j * D:(j + 1) * D], ident[:, :])
                mm.then_inc(t_done, 1)

            def layer1(it, off, qd):
                m = Q * off + qd
                if qd == 0:
                    wait(pe, kt_copied, it, RING * NT, NT * (off + 1))
                    wait(pe, we_ready, it, RING, off + 1)
                wait(pe, relu1_done, it, RING * Q, m - 1)
                for u in range(PAIRS):
                    for half in range(2):
                        i = QR * qd + 2 * u + half
                        mm = pe.matmul(ps_1[m % 2][half * H:(half + 1) * H, u * S:(u + 1) * S],
                                       we[:, off % 2, i, :], kt[:, off % 2, :, R * i:R * (i + 1)],
                                       start=True, stop=True)
                mm.then_inc(l1_done, 1)

            def layer2(it, m):
                wait(pe, relu1_done, it, RING * Q, m + 1)
                wait(pe, relu2_done, it, RING * Q, m - 1)
                pe.matmul(ps_2[m % 2][:, 0:QT], w2_sb[:, :], h1[:, m % 2, :],
                          start=True, stop=True).then_inc(l2_done, 1)

            def layer3(it, off):
                wait(pe, relu2_done, it, RING * Q, Q * (off + 1))
                c = off % GC
                if c == 0:
                    wait(pe, scores_copied, it, GI, off // GC)
                for u in range(PAIRS):
                    for q in range(Q):
                        mm = pe.matmul(ps_s[32 * q:32 * q + 32, 0:S], w3_sb[:, PAIRS * c + u, :],
                                       h2[:, off % 2, PAIRS * q + u, :],
                                       start=(c == 0 and u == 0), stop=(c == GC - 1 and u == PAIRS - 1))
                mm.then_inc(l3_done, 1)

            def weighted_sum(it, gl, js):
                par = gl % 2
                if js[0] == 0:
                    wait(pe, pw_ready, it, GI, gl + 1)
                    wait(pe, out_ready, it, GI, gl)
                for j in js:
                    for c in range(GC):
                        p0 = 64 * (j % 2) + 32 * c
                        slot = (GC * gl + c) % RING
                        mm = pe.matmul(ps_o[p0:p0 + CB, 0:D], pw[:, par, c, j, :], ring[:, slot, j * D:(j + 1) * D],
                                       start=(j < 2), stop=(j >= J - 2))
                if js[-1] == J - 1:
                    mm.then_inc(out_done, 1)

            TQ = [[0, 1], [2, 3], [4, 5], [6]]
            JQ = [range(0, 7), range(7, 13), range(13, 19), range(19, J)]

            def body(it, sl):
                for qd in range(Q):
                    if real(it, sl, NCH, RING):
                        for t in TQ[qd]:
                            transposes(it, sl, t)
                    if real(it, sl - 1, NCH, RING):
                        layer1(it, sl - 1, qd)
                    m = Q * (sl - 1) + qd - 1
                    if real(it, m, NCH * Q, RING * Q):
                        layer2(it, m)
                    if qd == 1 and real(it, sl - 2, NCH, RING):
                        layer3(it, sl - 2)
                    gl = (sl - 5) // GC
                    if sl % GC == 1 and real(it, gl, NG, GI):
                        weighted_sum(it, gl, JQ[qd])

            steps(pe, body)

        @block.vector
        def _(dve):
            nc.vector.memset(ring[:, RING - 4:RING, :].rearrange("p a f -> p (a f)"), 0.0).then_inc(stage_cleared, 1)
            nc.vector.memset(w2_sb[0:H, H:P], 0.0).then_inc(consts, 1)
            nc.vector.memset(w2_sb[H:P, 0:H], 0.0).then_inc(consts, 1)
            nc.vector.memset(w3_sb[:, :, :], 0.0).then_inc(w1_ready, 1)
            nc.vector.memset(neg[:, :], NEG_INF)
            nc.vector.memset(ps_o[:, :], 0.0)
            dve.wait_ge(query_loaded, 32)
            nc.vector.tensor_tensor(w_query[:, :], w1_sb[:, 0, :], w1_sb[:, 2, :], ALU.add)
            nc.vector.tensor_tensor(w_key[:, :], w1_sb[:, 1, :], w1_sb[:, 2, :], ALU.subtract).then_inc(w1_ready, 1)
            for n in range(B // P // 4):
                dve.wait_ge(q_transposed, n + 1)
                nc.vector.tensor_copy(qt[:, 512 * n:512 * (n + 1)], ps_t[n % 2][:, :]).then_inc(q_copied, 1)
            dve.wait_ge(weights_loaded, 16 * 9)
            dve.wait_ge(w1_ready, 1)
            for c in range(GC):
                for u in range(PAIRS):
                    for half in range(2):
                        col = QR * c + 2 * u + half
                        ins = nc.vector.tensor_copy(w3_sb[half * H:(half + 1) * H, PAIRS * c + u, col:col + 1],
                                                    w3_col[half * H:(half + 1) * H, :])
            ins.then_inc(consts, 1)
            dve.wait_ge(mask_loaded, 16 * 2 * Q * GC)
            nc.vector.tensor_scalar(dropped[:, :, :], mstage, 0, None, ALU.is_equal).then_inc(mask_done, 1)

            def copy_keys(it, sl, t):
                n = NT * sl + t
                wait(dve, t_done, it, RING * NT, n + 1)
                if t == 0:
                    wait(dve, l1_done, it, RING * Q, Q * (sl - 1))
                w = TSPLIT[t]
                nc.vector.tensor_copy(kt[:, sl % 2, TSTART[t]:TSTART[t] + w, :],
                                      ps_t[n % 2][:, 0:w * P].rearrange("p (a b) -> p a b", b=P)).then_inc(kt_copied, 1)

            def mask_and_max(it, gl):
                par = gl % 2
                nc.vector.copy_predicated(sc[:, par, :], drop[:, par, :], neg[:, :]).then_inc(masked, 1)
                wait(dve, masked, it, GI, gl + 1)
                nc.vector.tensor_reduce(nmax[:, par:par + 1], sc[:, par, :], AX.X, ALU.max, negate=True).then_inc(max_ready, 1)

            def normalize(it, gl):
                par = gl % 2
                wait(dve, exp_done, it, GI, gl + 1)
                nc.vector.reciprocal(rinv[:, par:par + 1], rsum[:, par:par + 1]).then_inc(rinv_ready, 1)
                wait(dve, rinv_ready, it, GI, gl + 1)
                nc.vector.tensor_scalar(pr[:, par, :], pr[:, par, :], rinv[:, par:par + 1], None,
                                        ALU.mult).then_inc(probs_ready, 1)

            def add_halves(it, gl):
                par = gl % 2
                wait(dve, half_copied, it, GI, gl + 1)
                wait(dve, stored[par], it, GI // 2 * 16 * GC, (gl // 2) * 16 * GC)
                nc.vector.tensor_tensor(osb[0:32 + CB, par, :], ps_o[0:32 + CB, 0:D], oh[0:32 + CB, :],
                                        ALU.add).then_inc(out_ready, 1)

            def body(it, sl):
                for t in range(NT):
                    if t == 5 and sl % GC == 1 and real(it, (sl - 3) // GC, NG, GI):
                        wait(dve, scores_copied, it, GI, (sl - 3) // GC + 1)
                        wait(dve, drop_ready, it, GI, (sl - 3) // GC + 1)
                    if real(it, sl, NCH, RING):
                        copy_keys(it, sl, t)
                    gl = (sl - 6) // GC
                    if t == 1 and sl % GC == 0 and real(it, gl, NG, GI):
                        add_halves(it, gl)
                    gl = (sl - 3) // GC
                    if t == 5 and sl % GC == 1 and real(it, gl, NG, GI):
                        mask_and_max(it, gl)
                if sl % GC == 1 and real(it, (sl - 3) // GC, NG, GI):
                    normalize(it, (sl - 3) // GC)

            steps(dve, body)


_INS = ["r_query", "r_keys", "r_mask", "L0_rec_W1", "L0_rec_b1", "L0_rec_W2", "L0_rec_b2", "L0_rec_W3", "L0_rec_b3"]


def kernel(**inputs):
    import numpy as _np
    import concourse.bacc as _bacc
    from concourse import mybir as _mybir
    from concourse.bass_utils import run_bass_kernel_spmd as _run

    nc = _bacc.Bacc("TRN2", target_bir_lowering=False, num_devices=1)
    arrays, args = {}, []
    for name in _INS:
        a = _np.ascontiguousarray(inputs[name])
        arrays[f"in_{name}"] = a
        args.append(nc.dram_tensor(f"in_{name}", a.shape, _mybir.dt.from_np(a.dtype), kind="ExternalInput").ap())
    b, _, d = inputs["r_keys"].shape
    out = nc.dram_tensor("out_0", (b, d), _mybir.dt.float32, kind="ExternalOutput").ap()
    din_attention(nc, *args, out)
    r = _run(nc, [arrays], core_ids=[0])
    return r.results[0]["out_0"]
```

```python
from contextlib import ExitStack

import concourse.bass as bass
from concourse import mybir
from concourse.alu_op_type import AluOpType as ALU

F32 = mybir.dt.float32
F32R = mybir.dt.float32r
I32 = mybir.dt.int32
U8 = mybir.dt.uint8
ACT = mybir.ActivationFunctionType
AX = mybir.AxisListType

P = 128
NEG_INF = -1000000000.0


def din_attention(nc, query, keys, mask, w1, b1, w2, b2, w3, b3, out):
    B, S, D = keys.shape
    H = w2.shape[0]
    CB = 16
    TOK = CB * S
    J = TOK // P
    R = P // CB
    NCH = B // CB
    GC = 2
    NG = NCH // GC
    RING = 8
    GI = RING // GC
    ITERS = NCH // RING
    Q = 4
    QR = CB // Q
    PAIRS = QR // 2
    QT = QR * S // 2
    TSPLIT = [4, 4, 4, 4, 3, 3, 3]
    NT = len(TSPLIT)
    TSTART = [sum(TSPLIT[:t]) for t in range(NT)]
    CONV = len(TSPLIT)
    LAST = NCH + 6
    SUMS = [(5, 1, range(0, 8)), (6, 0, range(8, 16)), (6, 1, range(16, J))]
    assert D == P and R * J == S and sum(TSPLIT) == J and 2 * H == P

    keys_c = keys.rearrange("(n i) s d -> n (i s d)", i=CB).rearrange("n (p f) -> n p f", p=P)
    mask_g = mask.rearrange("(h g c q v) s -> h q c v g s", h=2, c=GC, q=Q, v=QR)
    out_g = out.rearrange("(g c i) d -> g c i d", c=GC, i=CB)

    with ExitStack() as ctx:
        def sb(name, shape, dt=F32):
            return ctx.enter_context(nc.sbuf_tensor(name, shape, dt))

        def ps(name):
            return ctx.enter_context(nc.psum_tensor(name, [P, 512], F32))

        def sem(name):
            return ctx.enter_context(nc.semaphore(name))

        ring = sb("ring", [P, RING, J * D])
        kt = sb("kt", [P, 2, J, P])
        we = sb("we", [P, 2, CB, H])
        h1 = sb("h1", [P, 2, QT])
        h1_hi = sb("h1_hi", [P, Q, QT], F32R)
        h1_lo = sb("h1_lo", [P, Q, QT], F32R)
        h2 = sb("h2", [P, 2, CB // 2, S])
        qt = sb("qt", [P, B])
        bias1 = sb("bias1", [P, B // 2])
        w1_sb = sb("w1_sb", [P, 4, H])
        w_key = sb("w_key", [P, H])
        w_query = sb("w_query", [P, H])
        w2_sb = sb("w2_sb", [P, P])
        w2_hi = sb("w2_hi", [P, P], F32R)
        w2_lo = sb("w2_lo", [P, P], F32R)
        w3_col = sb("w3_col", [P, 1])
        w3_sb = sb("w3_sb", [P, GC * PAIRS, 32])
        b1_sb = sb("b1_sb", [P, 1])
        b2_sb = sb("b2_sb", [P, 1])
        b3_sb = sb("b3_sb", [P, 1])
        ident = sb("ident", [P, P])
        own = sb("own", [P, CB])
        dropped = sb("dropped", [P, NG, S], U8)
        drop = sb("drop", [P, 2, S], U8)
        neg = sb("neg", [P, S])
        sc = sb("sc", [P, 2, S])
        pr = sb("pr", [P, 2, S])
        nmax = sb("nmax", [P, 2])
        rsum = sb("rsum", [P, 2])
        rinv = sb("rinv", [P, 2])
        pn = sb("pn", [P, 2, GC, J])
        pw = sb("pw", [P, 2, GC, J, CB])
        oh = sb("oh", [P, D])
        osb = sb("osb", [P, 2, D])
        q_nat = h2[:, :, :, :].rearrange("p a b s -> p (a b s)")[:, 0:B // P * D].rearrange(
            "p (n d) -> p n d", d=D)
        mstage = ring[:, RING - 4:RING, :].rearrange("p a f -> p (a f)").bitcast(I32)[:, :].rearrange(
            "p (g s) -> p g s", s=S)

        ps_t = [ps("ps_t0"), ps("ps_t1")]
        ps_1 = [ps("ps_10"), ps("ps_11")]
        ps_2 = [ps("ps_20"), ps("ps_21")]
        ps_s = ps("ps_s")
        ps_o = ps("ps_o")

        query_loaded = sem("query_loaded")
        weights_loaded = sem("weights_loaded")
        w2_cleared = sem("w2_cleared")
        stage_cleared = sem("stage_cleared")
        stage_cleared2 = sem("stage_cleared2")
        mask_loaded = sem("mask_loaded")
        mask_done = sem("mask_done")
        keys_loaded = [sem(f"keys_loaded{i}") for i in range(RING)]
        ident_ready = sem("ident_ready")
        consts = sem("consts")
        pool_chain = sem("pool_chain")
        w1_ready = sem("w1_ready")
        q_transposed = sem("q_transposed")
        q_copied = sem("q_copied")
        qw_done = sem("qw_done")
        bias1_ready = sem("bias1_ready")
        t_done = sem("t_done")
        kt_copied = sem("kt_copied")
        we_ready = sem("we_ready")
        we_mult = sem("we_mult")
        drop_ready = sem("drop_ready")
        l1_done = sem("l1_done")
        relu1_done = sem("relu1_done")
        hi_done = sem("hi_done")
        lo_done = sem("lo_done")
        l2_done = sem("l2_done")
        relu2_done = sem("relu2_done")
        l3_done = sem("l3_done")
        scores_copied = sem("scores_copied")
        masked = sem("masked")
        max_ready = sem("max_ready")
        exp_done = sem("exp_done")
        rinv_ready = sem("rinv_ready")
        probs_ready = sem("probs_ready")
        spread = [sem(f"spread{i}") for i in range(2)]
        pw_ready = sem("pw_ready")
        out_done = sem("out_done")
        half_copied = sem("half_copied")
        out_ready = sem("out_ready")
        stored = [sem(f"stored{i}") for i in range(2)]

        def wait(eng, s, it, per, const):
            v = it * per + const
            if not isinstance(v, int) or v > 0:
                eng.wait_ge(s, v)

        def steps(eng, body):
            for sl in range(RING):
                body(0, sl)
            with eng.Fori(1, ITERS) as it:
                for sl in range(RING):
                    body(it, sl)
            for sl in range(LAST - NCH):
                body(ITERS, sl)

        def real(it, off, n, per):
            return not isinstance(it, int) or 0 <= it * per + off < n

        block = ctx.enter_context(nc.Block())

        @block.sync
        def _(sp):
            sp.dma_start(q_nat, query.rearrange("(n p) d -> p n d", p=P)).then_inc(query_loaded, 16)
            sp.dma_start(w1_sb[:, :, :], w1.rearrange("(b d) h -> d b h", d=D)).then_inc(query_loaded, 16)

            def index(v):
                return v if isinstance(v, int) else sp.snap(v)

            def load(n, sl):
                sp.dma_start(ring[:, sl, :], keys_c[n]).then_inc(keys_loaded[sl], 16)

            load(0, 0)
            sp.wait_ge(weights_loaded, 16 * 9)
            for sl in range(1, RING - 4):
                load(sl, sl)
            sp.wait_ge(stage_cleared, 1)
            sp.wait_ge(stage_cleared2, 1)
            for half in range(2):
                for q in range(Q):
                    for c in range(GC):
                        p0 = 32 * q + QR * c
                        sp.dma_start(mstage[p0:p0 + QR, half * NG // 2:(half + 1) * NG // 2, :],
                                     mask_g[half, q, c]).then_inc(mask_loaded, 16)
            sp.wait_ge(mask_done, CONV)
            for sl in range(RING - 4, RING):
                load(sl, sl)

            def store(it, gl):
                par = gl % 2
                g = index(it * GI + gl)
                wait(sp, out_ready, it, GI, gl + 1)
                for c in range(GC):
                    sp.dma_start(out_g[g, c], osb[32 * c:32 * c + CB, par, :]).then_inc(stored[par], 16)

            def group(it, gl, first=False, loads=True):
                par = gl % 2
                wait(sp, probs_ready, it, GI, gl + 1)
                for q in range(Q):
                    for c in range(GC):
                        p0 = 32 * q + QR * c
                        sp.dma_start(pn[32 * q:32 * q + 32, par, c, :],
                                     pr[p0:p0 + QR, par, :].rearrange("v (r j) -> v r j", j=J)
                                     ).then_inc(spread[par], 16)
                if first:
                    return
                n = [it * RING + GC * gl + RING - GC + c for c in range(GC)]
                if loads:
                    n = [index(v) for v in n]
                wait(sp, out_done, it, GI, gl)
                for c in range(GC):
                    if loads:
                        load(n[c], (GC * gl + RING - GC + c) % RING)
                store(it, gl - 1)

            for gl in range(GI):
                group(0, gl, first=gl == 0)
            with sp.Fori(1, ITERS - 1) as it:
                for gl in range(GI):
                    group(it, gl)
            for gl in range(GI):
                group(ITERS - 1, gl, loads=gl == 0)
            store(ITERS - 1, GI - 1)
            for par in range(2):
                sp.wait_ge(stored[par], 16 * GC * NG // 2)

        @block.gpsimd
        def _(pool):
            nc.gpsimd.memset(ident[:, :], 0.0).then_inc(pool_chain, 1)
            nc.gpsimd.memset(own[:, :], 1.0).then_inc(pool_chain, 1)
            pool.wait_ge(pool_chain, 2)
            nc.gpsimd.affine_select(out=ident[:, :], in_=ident[:, :], compare_op=ALU.not_equal, fill=1.0,
                                    base=0, pattern=[[-1, P]], channel_multiplier=1).then_inc(ident_ready, 1)
            nc.gpsimd.memset(ring[:, RING - 2:RING, :].rearrange("p a f -> p (a f)"), 0.0).then_inc(stage_cleared2, 1)
            nc.gpsimd.affine_select(out=own[:, :], in_=own[:, :], compare_op=ALU.is_ge, fill=0.0,
                                    base=0, pattern=[[-R, CB]], channel_multiplier=1).then_inc(pool_chain, 1)
            pool.wait_ge(pool_chain, 3)
            nc.gpsimd.affine_select(out=own[:, :], in_=own[:, :], compare_op=ALU.is_ge, fill=0.0,
                                    base=R - 1, pattern=[[R, CB]], channel_multiplier=-1).then_inc(pool_chain, 1)
            pool.wait_ge(pool_chain, 4)
            pool.wait_ge(w1_ready, 2)
            pool.wait_ge(q_copied, 4)

            def weights(it, off):
                par = off % 2
                if isinstance(it, int):
                    qc = qt[:, (it * RING + off) * CB:(it * RING + off + 1) * CB]
                else:
                    qc = qt[:, bass.ds(it * (RING * CB) + off * CB, CB)]
                wait(pool, l1_done, it, RING * Q, Q * (off - 1))
                nc.gpsimd.tensor_tensor(we[:, par], w1_sb[:, 3:4, :].to_broadcast([P, CB, H]),
                                        qc.unsqueeze(2).to_broadcast([P, CB, H]), ALU.mult).then_inc(we_mult, 1)
                wait(pool, we_mult, it, RING, off + 1)
                nc.gpsimd.tensor_tensor(we[:, par], we[:, par], w_key[:, :].unsqueeze(1).to_broadcast([P, CB, H]),
                                        ALU.add).then_inc(we_ready, 1)

            def spread_probs(it, gl, par):
                wait(pool, spread[par], it, GI // 2 * 16 * Q * GC, (gl // 2 + 1) * 16 * Q * GC)
                wait(pool, out_done, it, GI, gl - 1)
                for c in range(GC):
                    ins = nc.gpsimd.tensor_tensor(pw[:, par, c], pn[:, par, c, :].unsqueeze(2).to_broadcast([P, J, CB]),
                                                  own[:, :].unsqueeze(1).to_broadcast([P, J, CB]), ALU.mult)
                ins.then_inc(pw_ready, 1)

            def take_mask(it, gl):
                if isinstance(it, int):
                    part = dropped[:, it * GI + gl, :]
                else:
                    part = dropped[:, bass.ds(it * GI + gl, 1), :].rearrange("p a s -> p (a s)")
                if isinstance(it, int) and it == 0 and gl == 0:
                    pool.wait_ge(mask_done, CONV)
                wait(pool, masked, it, GI, gl - 1)
                nc.gpsimd.tensor_copy(drop[:, gl % 2, :], part).then_inc(drop_ready, 1)

            def body(it, sl):
                if real(it, sl, NCH, RING):
                    weights(it, sl)
                gl = (sl - 3) // GC
                if sl % GC == 1 and real(it, gl, NG, GI):
                    take_mask(it, gl)
                gl = (sl - 4) // GC
                if sl % GC == 0 and real(it, gl, NG, GI):
                    spread_probs(it, gl, gl % 2)

            steps(pool, body)

        @block.scalar
        def _(act):
            act.wait_ge(w2_cleared, 1)
            act.dma_start(w2_sb[0:H, 0:H], w2).then_inc(weights_loaded, 16)
            act.dma_start(w2_sb[H:P, H:P], w2).then_inc(weights_loaded, 16)
            for half in range(2):
                p0 = half * H
                act.dma_start(w3_col[p0:p0 + H, :], w3).then_inc(weights_loaded, 16)
                act.dma_start(b1_sb[p0:p0 + H, :], b1.rearrange("(h a) -> h a", a=1)).then_inc(weights_loaded, 16)
                act.dma_start(b2_sb[p0:p0 + H, :], b2.rearrange("(h a) -> h a", a=1)).then_inc(weights_loaded, 16)
            act.dma_start(b3_sb[:, :], b3.rearrange("(h a) -> h a", a=1).to_broadcast([P, 1])).then_inc(weights_loaded, 16)
            act.wait_ge(weights_loaded, 16 * 9)
            for n in range(B // 2 // 512):
                act.wait_ge(qw_done, n + 1)
                nc.scalar.activation(bias1[:, 512 * n:512 * (n + 1)], ps_1[n % 2][:, :], ACT.Identity,
                                     bias=b1_sb[:, :]).then_inc(bias1_ready, 1)
            act.wait_ge(bias1_ready, B // 2 // 512)

            def relu1(it, m):
                wait(act, l1_done, it, RING * Q, m + 1)
                wait(act, lo_done, it, RING * Q, m - 1)
                for u in range(PAIRS):
                    if isinstance(it, int):
                        pair = (it * RING * Q + m) * PAIRS + u
                        bias = bias1[:, pair:pair + 1]
                    else:
                        bias = bias1[:, bass.ds(it * (RING * Q * PAIRS) + m * PAIRS + u, 1)]
                    ins = nc.scalar.activation(h1[:, m % 2, u * S:(u + 1) * S], ps_1[m % 2][:, u * S:(u + 1) * S],
                                               ACT.Relu, bias=bias)
                ins.then_inc(relu1_done, 1)

            def high_part(it, m):
                wait(act, relu1_done, it, RING * Q, m + 1)
                nc.scalar.activation(h1_hi[:, m % Q, :], h1[:, m % 2, :], ACT.Copy).then_inc(hi_done, 1)

            def relu2(it, m):
                wait(act, l2_done, it, RING * Q, m + 1)
                off = m // Q
                if m % Q == 0:
                    wait(act, l3_done, it, RING, off - 1)
                nc.scalar.activation(h2[:, off % 2, PAIRS * (m % Q):PAIRS * (m % Q + 1), :],
                                     ps_2[m % 2][:, 0:QT].rearrange("p (u s) -> p u s", s=S),
                                     ACT.Relu, bias=b2_sb[:, :]).then_inc(relu2_done, 1)

            def copy_scores(it, gl):
                wait(act, l3_done, it, RING, GC * (gl + 1))
                wait(act, exp_done, it, GI, gl - 1)
                nc.scalar.activation(sc[:, gl % 2, :].rearrange("p (r j) -> p r j", j=J),
                                     ps_s[:, 0:S].rearrange("p (j r) -> p r j", r=R),
                                     ACT.Identity, bias=b3_sb[:, :]).then_inc(scores_copied, 1)

            def exps(it, gl):
                par = gl % 2
                wait(act, max_ready, it, GI, gl + 1)
                wait(act, spread[par], it, GI // 2 * 16 * Q * GC, (gl // 2) * 16 * Q * GC)
                nc.scalar.activation(pr[:, par, :], sc[:, par, :], ACT.Exp, bias=nmax[:, par:par + 1],
                                     accum_out=rsum[:, par:par + 1]).then_inc(exp_done, 1)

            def copy_half(it, gl):
                wait(act, out_done, it, GI, gl + 1)
                wait(act, out_ready, it, GI, gl)
                nc.scalar.activation(oh[0:32 + CB, :], ps_o[64:96 + CB, 0:D], ACT.Copy).then_inc(half_copied, 1)

            def body(it, sl):
                for half in range(2):
                    m = Q * (sl - 1) + 2 * half
                    fresh = real(it, sl - 1, NCH, RING)
                    before = real(it, m - 2, NCH * Q, RING * Q)
                    softmax = sl % GC == 1 and half == 1 and real(it, (sl - 3) // GC, NG, GI)
                    if fresh:
                        relu1(it, m)
                        relu1(it, m + 1)
                    if sl % GC == 1 and half == 0 and real(it, (sl - 7) // GC, NG, GI):
                        copy_half(it, (sl - 7) // GC)
                    if fresh:
                        high_part(it, m)
                    if softmax:
                        copy_scores(it, (sl - 3) // GC)
                    if before:
                        relu2(it, m - 2)
                        relu2(it, m - 1)
                    if fresh:
                        high_part(it, m + 1)
                    if softmax:
                        exps(it, (sl - 3) // GC)

            steps(act, body)

        @block.tensor
        def _(pe):
            pe.wait_ge(ident_ready, 1)
            pe.wait_ge(query_loaded, 32)
            for n in range(B // P // 4):
                if n >= 2:
                    pe.wait_ge(q_copied, n - 1)
                for t in range(4):
                    mm = pe.transpose(ps_t[n % 2][:, t * P:(t + 1) * P], q_nat[:, 4 * n + t, :], ident[:, :])
                mm.then_inc(q_transposed, 1)
            pe.wait_ge(w1_ready, 2)
            pe.wait_ge(q_copied, B // P // 4)
            for n in range(B // 2 // 512):
                for half in range(2):
                    mm = pe.matmul(ps_1[n % 2][half * H:(half + 1) * H, :], w_query[:, :],
                                   qt[:, 1024 * n + half:1024 * (n + 1):2], start=True, stop=True)
                mm.then_inc(qw_done, 1)
            pe.wait_ge(bias1_ready, B // 2 // 512)
            pe.wait_ge(weights_loaded, 16 * 9)
            pe.wait_ge(consts, 3)


            def transposes(it, sl, t):
                n = NT * sl + t
                if t == 0:
                    pe.wait_ge(keys_loaded[sl], (it + 1) * 16)
                wait(pe, kt_copied, it, RING * NT, n - 1)
                for a in range(TSPLIT[t]):
                    j = TSTART[t] + a
                    mm = pe.transpose(ps_t[n % 2][:, a * P:(a + 1) * P], ring[:, sl, j * D:(j + 1) * D], ident[:, :])
                mm.then_inc(t_done, 1)

            def layer1(it, m):
                off = m // Q
                if m % Q == 0:
                    wait(pe, kt_copied, it, RING * NT, NT * (off + 1))
                    wait(pe, we_ready, it, RING, off + 1)
                wait(pe, relu1_done, it, RING * Q, m)
                for n in (m, m + 1):
                    for u in range(PAIRS):
                        for half in range(2):
                            i = QR * (n % Q) + 2 * u + half
                            mm = pe.matmul(ps_1[n % 2][half * H:(half + 1) * H, u * S:(u + 1) * S],
                                           we[:, off % 2, i, :], kt[:, off % 2, :, R * i:R * (i + 1)],
                                           start=True, stop=True)
                    mm.then_inc(l1_done, 1)

            def layer2(it, m, between):
                wait(pe, lo_done, it, RING * Q, m + 2)
                for k in (m, m + 1):
                    bank, n = ps_2[k % 2][:, 0:QT], k % Q
                    pe.matmul(bank, w2_hi[:, :], h1_hi[:, n, :], start=True, stop=False)
                    pe.matmul(bank, w2_hi[:, :], h1_lo[:, n, :], start=False, stop=False)
                    pe.matmul(bank, w2_lo[:, :], h1_hi[:, n, :], start=False, stop=True).then_inc(l2_done, 1)
                    if k == m:
                        between()

            def layer3(it, off):
                wait(pe, relu2_done, it, RING * Q, Q * (off + 1))
                c = off % GC
                if c == 0:
                    wait(pe, scores_copied, it, GI, off // GC)
                for u in range(PAIRS):
                    for q in range(Q):
                        mm = pe.matmul(ps_s[32 * q:32 * q + 32, 0:S], w3_sb[:, PAIRS * c + u, :],
                                       h2[:, off % 2, PAIRS * q + u, :],
                                       start=(c == 0 and u == 0), stop=(c == GC - 1 and u == PAIRS - 1))
                mm.then_inc(l3_done, 1)

            def weighted_sum(it, gl, js):
                par = gl % 2
                if js[0] == 0:
                    wait(pe, pw_ready, it, GI, gl + 1)
                    wait(pe, out_ready, it, GI, gl)
                for j in js:
                    for c in range(GC):
                        p0 = 64 * (j % 2) + 32 * c
                        slot = (GC * gl + c) % RING
                        mm = pe.matmul(ps_o[p0:p0 + CB, 0:D], pw[:, par, c, j, :], ring[:, slot, j * D:(j + 1) * D],
                                       start=(j < 2), stop=(j >= J - 2))
                if js[-1] == J - 1:
                    mm.then_inc(out_done, 1)

            def body(it, sl):
                for half in range(2):
                    m = Q * (sl - 1) + 2 * half
                    tiles = [0, 1, 2, 3] if half == 0 else [4, 5, 6]

                    def transpose_next():
                        if tiles and real(it, sl, NCH, RING):
                            transposes(it, sl, tiles.pop(0))

                    if half == 0:
                        transpose_next()
                    if real(it, sl - 1, NCH, RING):
                        layer1(it, m)
                    if half == 1:
                        transpose_next()
                    if half == 1 and real(it, sl - 2, NCH, RING):
                        layer3(it, sl - 2)
                    transpose_next()
                    if real(it, m - 2, NCH * Q, RING * Q):
                        layer2(it, m - 2, transpose_next)
                    else:
                        transpose_next()
                    for (step, h, js) in SUMS:
                        if half == h and sl % GC == step % GC and real(it, (sl - step) // GC, NG, GI):
                            weighted_sum(it, (sl - step) // GC, js)
                    transpose_next()

            steps(pe, body)

        @block.vector
        def _(dve):
            nc.vector.memset(w2_sb[:, :], 0.0).then_inc(w2_cleared, 1)
            nc.vector.memset(w3_sb[:, :, :], 0.0).then_inc(w1_ready, 1)
            nc.vector.memset(neg[:, :], NEG_INF)
            nc.vector.memset(ps_o[:, :], 0.0)
            nc.vector.memset(ring[:, RING - 4:RING - 2, :].rearrange("p a f -> p (a f)"), 0.0).then_inc(stage_cleared, 1)
            dve.wait_ge(query_loaded, 32)
            nc.vector.tensor_tensor(w_query[:, :], w1_sb[:, 0, :], w1_sb[:, 2, :], ALU.add)
            nc.vector.tensor_tensor(w_key[:, :], w1_sb[:, 1, :], w1_sb[:, 2, :], ALU.subtract).then_inc(w1_ready, 1)
            for n in range(B // P // 4):
                dve.wait_ge(q_transposed, n + 1)
                nc.vector.tensor_copy(qt[:, 512 * n:512 * (n + 1)], ps_t[n % 2][:, :]).then_inc(q_copied, 1)
            dve.wait_ge(weights_loaded, 16 * 9)
            dve.wait_ge(w1_ready, 1)
            for c in range(GC):
                for u in range(PAIRS):
                    for half in range(2):
                        col = QR * c + 2 * u + half
                        ins = nc.vector.tensor_copy(w3_sb[half * H:(half + 1) * H, PAIRS * c + u, col:col + 1],
                                                    w3_col[half * H:(half + 1) * H, :])
            ins.then_inc(consts, 1)
            nc.vector.tensor_copy(w2_hi[:, :], w2_sb[:, :]).then_inc(consts, 1)
            dve.wait_ge(consts, 2)
            nc.vector.tensor_tensor(w2_lo[:, :], w2_sb[:, :], w2_hi[:, :].bitcast(F32), ALU.subtract).then_inc(consts, 1)

            def convert_mask(n):
                part = slice(n * NG // CONV, (n + 1) * NG // CONV)
                dve.wait_ge(mask_loaded, 16 * 2 * Q * GC)
                nc.vector.tensor_scalar(dropped[:, part, :], mstage[:, part, :], 0, None, ALU.is_equal).then_inc(mask_done, 1)

            def copy_keys(it, sl, t):
                n = NT * sl + t
                wait(dve, t_done, it, RING * NT, n + 1)
                if t == 0:
                    wait(dve, l1_done, it, RING * Q, Q * (sl - 1))
                w = TSPLIT[t]
                nc.vector.tensor_copy(kt[:, sl % 2, TSTART[t]:TSTART[t] + w, :],
                                      ps_t[n % 2][:, 0:w * P].rearrange("p (a b) -> p a b", b=P)).then_inc(kt_copied, 1)

            def low_part(it, m):
                wait(dve, hi_done, it, RING * Q, m + 1)
                nc.vector.tensor_tensor(h1_lo[:, m % Q, :], h1[:, m % 2, :], h1_hi[:, m % Q, :].bitcast(F32),
                                        ALU.subtract).then_inc(lo_done, 1)

            def mask_and_max(it, gl):
                par = gl % 2
                nc.vector.copy_predicated(sc[:, par, :], drop[:, par, :], neg[:, :]).then_inc(masked, 1)
                wait(dve, masked, it, GI, gl + 1)
                nc.vector.tensor_reduce(nmax[:, par:par + 1], sc[:, par, :], AX.X, ALU.max, negate=True).then_inc(max_ready, 1)

            def normalize(it, gl):
                par = gl % 2
                wait(dve, exp_done, it, GI, gl + 1)
                nc.vector.reciprocal(rinv[:, par:par + 1], rsum[:, par:par + 1]).then_inc(rinv_ready, 1)
                wait(dve, rinv_ready, it, GI, gl + 1)
                nc.vector.tensor_scalar(pr[:, par, :], pr[:, par, :], rinv[:, par:par + 1], None,
                                        ALU.mult).then_inc(probs_ready, 1)

            def add_halves(it, gl):
                par = gl % 2
                wait(dve, half_copied, it, GI, gl + 1)
                wait(dve, stored[par], it, GI // 2 * 16 * GC, (gl // 2) * 16 * GC)
                nc.vector.tensor_tensor(osb[0:32 + CB, par, :], ps_o[0:32 + CB, 0:D], oh[0:32 + CB, :],
                                        ALU.add).then_inc(out_ready, 1)

            def body(it, sl):
                for t in range(NT):
                    new = real(it, sl, NCH, RING)
                    m = Q * (sl - 1) + (0 if t < 4 else 2)
                    softmax = sl % GC == 1 and real(it, (sl - 3) // GC, NG, GI)
                    if t == 6 and softmax:
                        wait(dve, scores_copied, it, GI, (sl - 3) // GC + 1)
                        wait(dve, drop_ready, it, GI, (sl - 3) // GC + 1)
                    if new:
                        copy_keys(it, sl, t)
                    if t == 6 and softmax:
                        mask_and_max(it, (sl - 3) // GC)
                    if t in (1, 2, 5, 6) and real(it, sl - 1, NCH, RING):
                        low_part(it, m + (t in (2, 6)))
                    if t == 0 and sl % GC == 0 and real(it, (sl - 4) // GC, NG, GI):
                        normalize(it, (sl - 4) // GC)
                    if t == 1 and sl % GC == 1 and real(it, (sl - 7) // GC, NG, GI):
                        add_halves(it, (sl - 7) // GC)
                    if isinstance(it, int) and it == 0 and sl == 2:
                        convert_mask(t)

            steps(dve, body)


_INS = ["r_query", "r_keys", "r_mask", "L0_rec_W1", "L0_rec_b1", "L0_rec_W2", "L0_rec_b2", "L0_rec_W3", "L0_rec_b3"]


def kernel(**inputs):
    import numpy as _np
    import concourse.bacc as _bacc
    from concourse import mybir as _mybir
    from concourse.bass_utils import run_bass_kernel_spmd as _run

    nc = _bacc.Bacc("TRN2", target_bir_lowering=False, num_devices=1)
    arrays, args = {}, []
    for name in _INS:
        a = _np.ascontiguousarray(inputs[name])
        arrays[f"in_{name}"] = a
        args.append(nc.dram_tensor(f"in_{name}", a.shape, _mybir.dt.from_np(a.dtype), kind="ExternalInput").ap())
    b, _, d = inputs["r_keys"].shape
    out = nc.dram_tensor("out_0", (b, d), _mybir.dt.float32, kind="ExternalOutput").ap()
    din_attention(nc, *args, out)
    r = _run(nc, [arrays], core_ids=[0])
    return r.results[0]["out_0"]
```

```python
from contextlib import ExitStack

import concourse.bass as bass
from concourse import mybir
from concourse.alu_op_type import AluOpType as ALU

F32 = mybir.dt.float32
F32R = mybir.dt.float32r
I32 = mybir.dt.int32
U8 = mybir.dt.uint8
ACT = mybir.ActivationFunctionType
AX = mybir.AxisListType

P = 128
NEG_INF = -1000000000.0


def din_attention(nc, query, keys, mask, w1, b1, w2, b2, w3, b3, out):
    B, S, D = keys.shape
    H = w2.shape[0]
    CB = 16
    TOK = CB * S
    J = TOK // P
    R = P // CB
    NCH = B // CB
    GC = 2
    NG = NCH // GC
    RING = 8
    GI = RING // GC
    ITERS = NCH // RING
    Q = 4
    QR = CB // Q
    PAIRS = QR // 2
    QT = QR * S // 2
    TSPLIT = [4, 4, 4, 4, 3, 3, 3]
    NT = len(TSPLIT)
    TSTART = [sum(TSPLIT[:t]) for t in range(NT)]
    ACT_T = 3
    CONV = len(TSPLIT)
    LAST = NCH + 7
    PE_SUMS = [(6, 0, range(0, 4)), (6, 1, range(4, 10))]
    DVE_SUMS = [(5, 3), (5, 3), (5, 4), (6, 1), (6, 2), (6, 3), (6, 3), (6, 4), (6, 6)]
    PE_SLOTS = PE_SUMS[-1][2][-1] + 1
    POOL_SLOTS = 6
    DVE_SLOTS = len(DVE_SUMS)
    assert PE_SLOTS + POOL_SLOTS + DVE_SLOTS == J
    assert D == P and R * J == S and sum(TSPLIT) == J and 2 * H == P

    keys_c = keys.rearrange("(n i) s d -> n (i s d)", i=CB).rearrange("n (p f) -> n p f", p=P)
    mask_g = mask.rearrange("(h g c i) s -> h c i g s", h=2, c=GC, i=CB)
    out_g = out.rearrange("(g c i) d -> g c i d", c=GC, i=CB)

    with ExitStack() as ctx:
        def sb(name, shape, dt=F32):
            return ctx.enter_context(nc.sbuf_tensor(name, shape, dt))

        def ps(name):
            return ctx.enter_context(nc.psum_tensor(name, [P, 512], F32))

        def sem(name):
            return ctx.enter_context(nc.semaphore(name))

        ring = sb("ring", [P, RING, J * D])
        kt = sb("kt", [P, 2, J, P])
        we = sb("we", [P, 2, CB, H])
        h1 = sb("h1", [P, 2, QT])
        h1_hi = sb("h1_hi", [P, Q, QT], F32R)
        h1_lo = sb("h1_lo", [P, Q, QT], F32R)
        h2 = sb("h2", [P, 2, CB // 2, S])
        qt = sb("qt", [P, B])
        bias1 = sb("bias1", [P, B // 2])
        w1_sb = sb("w1_sb", [P, 4, H])
        w_key = sb("w_key", [P, H])
        w_query = sb("w_query", [P, H])
        w2_sb = sb("w2_sb", [P, P])
        w2_hi = sb("w2_hi", [P, P], F32R)
        w2_lo = sb("w2_lo", [P, P], F32R)
        w3_col = sb("w3_col", [P, 1])
        w3_sb = sb("w3_sb", [P, GC * PAIRS, 32])
        b1_sb = sb("b1_sb", [P, 1])
        b2_sb = sb("b2_sb", [P, 1])
        b3_sb = sb("b3_sb", [P, 1])
        ident = sb("ident", [P, P])
        own = sb("own", [P, CB])
        dropped = sb("dropped", [P, NG, S], U8)
        drop = sb("drop", [P, 2, S], U8)
        neg = sb("neg", [P, S])
        sc = sb("sc", [P, 2, S])
        pr = sb("pr", [P, 2, S])
        nmax = sb("nmax", [P, 2])
        rsum = sb("rsum", [P, 2])
        rinv = sb("rinv", [P, 2])
        pn = sb("pn", [P, 2, GC, J])
        pw = sb("pw", [P, 2, GC, PE_SLOTS, CB])
        weighted = sb("weighted", [P, GC, POOL_SLOTS, D])
        part_sum = sb("part_sum", [P, 2, GC, D])
        oh = sb("oh", [P, D])
        osb = sb("osb", [P, 2, D])
        q_nat = h2[:, :, :, :].rearrange("p a b s -> p (a b s)")[:, 0:B // P * D].rearrange(
            "p (n d) -> p n d", d=D)
        mstage = ring[:, RING - 4:RING, :].rearrange("p a f -> p (a f)").bitcast(I32)[:, :].rearrange(
            "p (g s) -> p g s", s=S)

        ps_t = [ps("ps_t0"), ps("ps_t1")]
        ps_1 = [ps("ps_10"), ps("ps_11")]
        ps_2 = [ps("ps_20"), ps("ps_21")]
        ps_s = ps("ps_s")
        ps_o = ps("ps_o")

        query_loaded = sem("query_loaded")
        weights_loaded = sem("weights_loaded")
        w2_cleared = sem("w2_cleared")
        stage_cleared_dve = sem("stage_cleared_dve")
        stage_cleared_pool = sem("stage_cleared_pool")
        mask_loaded = sem("mask_loaded")
        mask_done = sem("mask_done")
        keys_loaded = [sem(f"keys_loaded{i}") for i in range(RING)]
        ident_ready = sem("ident_ready")
        consts = sem("consts")
        pool_chain = sem("pool_chain")
        w1_ready = sem("w1_ready")
        q_transposed = sem("q_transposed")
        q_copied = sem("q_copied")
        qw_done = sem("qw_done")
        bias1_ready = sem("bias1_ready")
        t_done = sem("t_done")
        kt_copied = sem("kt_copied")
        act_copied = sem("act_copied")
        we_ready = sem("we_ready")
        we_mult = sem("we_mult")
        drop_ready = sem("drop_ready")
        l1_done = sem("l1_done")
        relu1_done = sem("relu1_done")
        hi_done = sem("hi_done")
        lo_done = sem("lo_done")
        l2_done = sem("l2_done")
        relu2_done = sem("relu2_done")
        l3_done = sem("l3_done")
        scores_copied = sem("scores_copied")
        masked = sem("masked")
        max_ready = sem("max_ready")
        exp_done = sem("exp_done")
        rinv_ready = sem("rinv_ready")
        probs_ready = sem("probs_ready")
        spread = [sem(f"spread{i}") for i in range(2)]
        pw_ready = sem("pw_ready")
        slots_summed = sem("slots_summed")
        pool_weighted = sem("pool_weighted")
        pool_halved = sem("pool_halved")
        pool_paired = sem("pool_paired")
        pool_added = sem("pool_added")
        dve_added = sem("dve_added")
        out_done = sem("out_done")
        half_copied = sem("half_copied")
        out_ready = sem("out_ready")
        stored = [sem(f"stored{i}") for i in range(2)]

        def wait(eng, s, it, per, const):
            v = it * per + const
            if not isinstance(v, int) or v > 0:
                eng.wait_ge(s, v)

        def steps(eng, body):
            for sl in range(RING):
                body(0, sl)
            with eng.Fori(1, ITERS) as it:
                for sl in range(RING):
                    body(it, sl)
            for sl in range(LAST - NCH):
                body(ITERS, sl)

        def real(it, off, n, per):
            return not isinstance(it, int) or 0 <= it * per + off < n

        def copies(sl, t):
            return (NT - 1) * sl + t - (t > ACT_T)

        def copy_bank(copy, sl, t):
            w = TSPLIT[t]
            return copy(kt[:, sl % 2, TSTART[t]:TSTART[t] + w, :],
                        ps_t[(NT * sl + t) % 2][:, 0:w * P].rearrange("p (a b) -> p a b", b=P))

        block = ctx.enter_context(nc.Block())

        @block.sync
        def _(sp):
            sp.dma_start(q_nat, query.rearrange("(n p) d -> p n d", p=P)).then_inc(query_loaded, 16)
            sp.dma_start(w1_sb[:, :, :], w1.rearrange("(b d) h -> d b h", d=D)).then_inc(query_loaded, 16)

            def index(v):
                return v if isinstance(v, int) else sp.snap(v)

            def load(n, sl):
                sp.dma_start(ring[:, sl, :], keys_c[n]).then_inc(keys_loaded[sl], 16)

            load(0, 0)
            sp.wait_ge(weights_loaded, 16 * 9)
            for sl in range(1, RING - 4):
                load(sl, sl)
            sp.wait_ge(stage_cleared_dve, 1)
            sp.wait_ge(stage_cleared_pool, 1)
            for half in range(2):
                for c in range(GC):
                    sp.dma_start(mstage[c::R, half * NG // 2:(half + 1) * NG // 2, :],
                                 mask_g[half, c]).then_inc(mask_loaded, 16)
            sp.wait_ge(mask_done, CONV)
            for sl in range(RING - 4, RING - 2):
                load(sl, sl)

            def store(it, gl):
                par = gl % 2
                g = index(it * GI + gl)
                wait(sp, out_ready, it, GI, gl + 1)
                for c in range(GC):
                    sp.dma_start(out_g[g, c], osb[32 * c:32 * c + CB, par, :]).then_inc(stored[par], 16)

            def group(it, gl, first=False, loads=True):
                par = gl % 2
                wait(sp, probs_ready, it, GI, gl + 1)
                for c in range(GC):
                    sp.dma_start(pn[:, par, c, :], pr[c::R, par, :].rearrange("i (r j) -> i r j", j=J)
                                 ).then_inc(spread[par], 16)
                if first:
                    return
                n = [it * RING + GC * gl + RING - GC + c for c in range(GC)]
                if loads:
                    n = [index(v) for v in n]
                    added = index((it * GI + gl) * GC * DVE_SLOTS)
                    summed = index(it * GI + gl)
                    sp.wait_ge(dve_added, added)
                    sp.wait_ge(slots_summed, summed)
                for c in range(GC):
                    if loads:
                        load(n[c], (GC * gl + RING - GC + c) % RING)
                store(it, gl - 1)

            group(0, 0, first=True)
            for sl in range(RING - 2, RING):
                load(sl, sl)
            for gl in range(1, GI):
                group(0, gl)
            with sp.Fori(1, ITERS - 1) as it:
                for gl in range(GI):
                    group(it, gl)
            for gl in range(GI):
                group(ITERS - 1, gl, loads=gl == 0)
            store(ITERS - 1, GI - 1)
            for par in range(2):
                sp.wait_ge(stored[par], 16 * GC * NG // 2)

        @block.gpsimd
        def _(pool):
            nc.gpsimd.memset(ident[:, :], 0.0).then_inc(pool_chain, 1)
            nc.gpsimd.memset(own[:, :], 1.0).then_inc(pool_chain, 1)
            pool.wait_ge(pool_chain, 2)
            nc.gpsimd.affine_select(out=ident[:, :], in_=ident[:, :], compare_op=ALU.not_equal, fill=1.0,
                                    base=0, pattern=[[-1, P]], channel_multiplier=1).then_inc(ident_ready, 1)
            nc.gpsimd.memset(ring[:, RING - 2:RING, :].rearrange("p a f -> p (a f)"), 0.0).then_inc(stage_cleared_pool, 1)
            nc.gpsimd.affine_select(out=own[:, :], in_=own[:, :], compare_op=ALU.is_ge, fill=0.0,
                                    base=0, pattern=[[-R, CB]], channel_multiplier=1).then_inc(pool_chain, 1)
            pool.wait_ge(pool_chain, 3)
            nc.gpsimd.affine_select(out=own[:, :], in_=own[:, :], compare_op=ALU.is_ge, fill=0.0,
                                    base=R - 1, pattern=[[R, CB]], channel_multiplier=-1).then_inc(pool_chain, 1)
            pool.wait_ge(pool_chain, 4)
            pool.wait_ge(w1_ready, 2)
            pool.wait_ge(q_copied, 4)

            def weights(it, off):
                par = off % 2
                if isinstance(it, int):
                    qc = qt[:, (it * RING + off) * CB:(it * RING + off + 1) * CB]
                else:
                    qc = qt[:, bass.ds(it * (RING * CB) + off * CB, CB)]
                wait(pool, l1_done, it, RING * Q, Q * (off - 1))
                nc.gpsimd.tensor_tensor(we[:, par], w1_sb[:, 3:4, :].to_broadcast([P, CB, H]),
                                        qc.unsqueeze(2).to_broadcast([P, CB, H]), ALU.mult).then_inc(we_mult, 1)
                wait(pool, we_mult, it, RING, off + 1)
                nc.gpsimd.tensor_tensor(we[:, par], we[:, par], w_key[:, :].unsqueeze(1).to_broadcast([P, CB, H]),
                                        ALU.add).then_inc(we_ready, 1)

            def spread_probs(it, gl, par):
                wait(pool, spread[par], it, GI // 2 * 16 * GC, (gl // 2 + 1) * 16 * GC)
                wait(pool, out_done, it, GI, gl - 1)
                for c in range(GC):
                    ins = nc.gpsimd.tensor_tensor(pw[:, par, c],
                                                  pn[:, par, c, 0:PE_SLOTS].unsqueeze(2).to_broadcast([P, PE_SLOTS, CB]),
                                                  own[:, :].unsqueeze(1).to_broadcast([P, PE_SLOTS, CB]), ALU.mult)
                ins.then_inc(pw_ready, 1)

            def add_slots(it, gl):
                par, js = gl % 2, slice(PE_SLOTS, PE_SLOTS + POOL_SLOTS)
                slot = GC * gl % RING
                keys_j = ring[:, slot:slot + GC, js.start * D:js.stop * D].rearrange("p c (j d) -> p c j d", d=D)
                nc.gpsimd.tensor_tensor(weighted[:, :, :, :], keys_j,
                                        pn[:, par, :, js].unsqueeze(3).to_broadcast([P, GC, POOL_SLOTS, D]),
                                        ALU.mult).then_inc(pool_weighted, 1)
                wait(pool, pool_weighted, it, GI, gl + 1)
                half = POOL_SLOTS // 2
                nc.gpsimd.tensor_tensor(weighted[:, :, 0:half, :], weighted[:, :, 0:half, :],
                                        weighted[:, :, half:, :], ALU.add).then_inc(pool_halved, 1)
                wait(pool, pool_halved, it, GI, gl + 1)
                nc.gpsimd.tensor_tensor(weighted[:, :, 0, :], weighted[:, :, 0, :], weighted[:, :, 1, :],
                                        ALU.add).then_inc(pool_paired, 1)
                wait(pool, pool_paired, it, GI, gl + 1)
                wait(pool, out_done, it, GI, gl - 1)
                nc.gpsimd.tensor_tensor(part_sum[:, par], weighted[:, :, 0, :], weighted[:, :, 2, :],
                                        ALU.add).then_inc(pool_added, 1)

            def take_mask(it, gl):
                if isinstance(it, int):
                    part = dropped[:, it * GI + gl, :]
                else:
                    part = dropped[:, bass.ds(it * GI + gl, 1), :].rearrange("p a s -> p (a s)")
                if isinstance(it, int) and it == 0 and gl == 0:
                    pool.wait_ge(mask_done, CONV)
                wait(pool, masked, it, GI, gl - 1)
                nc.gpsimd.tensor_copy(drop[:, gl % 2, :], part).then_inc(drop_ready, 1)

            def body(it, sl):
                if real(it, sl, NCH, RING):
                    weights(it, sl)
                gl = (sl - 3) // GC
                if sl % GC == 1 and real(it, gl, NG, GI):
                    take_mask(it, gl)
                gl = (sl - 4) // GC
                if sl % GC == 0 and real(it, gl, NG, GI):
                    spread_probs(it, gl, gl % 2)
                    add_slots(it, gl)

            steps(pool, body)

        @block.scalar
        def _(act):
            act.wait_ge(w2_cleared, 1)
            act.dma_start(w2_sb[0:H, 0:H], w2).then_inc(weights_loaded, 16)
            act.dma_start(w2_sb[H:P, H:P], w2).then_inc(weights_loaded, 16)
            for half in range(2):
                p0 = half * H
                act.dma_start(w3_col[p0:p0 + H, :], w3).then_inc(weights_loaded, 16)
                act.dma_start(b1_sb[p0:p0 + H, :], b1.rearrange("(h a) -> h a", a=1)).then_inc(weights_loaded, 16)
                act.dma_start(b2_sb[p0:p0 + H, :], b2.rearrange("(h a) -> h a", a=1)).then_inc(weights_loaded, 16)
            act.dma_start(b3_sb[:, :], b3.rearrange("(h a) -> h a", a=1).to_broadcast([P, 1])).then_inc(weights_loaded, 16)
            act.wait_ge(weights_loaded, 16 * 9)
            for n in range(B // 2 // 512):
                act.wait_ge(qw_done, n + 1)
                nc.scalar.activation(bias1[:, 512 * n:512 * (n + 1)], ps_1[n % 2][:, :], ACT.Identity,
                                     bias=b1_sb[:, :]).then_inc(bias1_ready, 1)
            act.wait_ge(bias1_ready, B // 2 // 512)

            def relu1(it, m):
                wait(act, l1_done, it, RING * Q, m + 1)
                wait(act, lo_done, it, RING * Q, m - 1)
                for u in range(PAIRS):
                    if isinstance(it, int):
                        pair = (it * RING * Q + m) * PAIRS + u
                        bias = bias1[:, pair:pair + 1]
                    else:
                        bias = bias1[:, bass.ds(it * (RING * Q * PAIRS) + m * PAIRS + u, 1)]
                    ins = nc.scalar.activation(h1[:, m % 2, u * S:(u + 1) * S], ps_1[m % 2][:, u * S:(u + 1) * S],
                                               ACT.Relu, bias=bias)
                ins.then_inc(relu1_done, 1)

            def high_part(it, m):
                wait(act, relu1_done, it, RING * Q, m + 1)
                nc.scalar.activation(h1_hi[:, m % Q, :], h1[:, m % 2, :], ACT.Copy).then_inc(hi_done, 1)

            def relu2(it, m):
                wait(act, l2_done, it, RING * Q, m + 1)
                off = m // Q
                if m % Q == 0:
                    wait(act, l3_done, it, RING, off - 1)
                nc.scalar.activation(h2[:, off % 2, PAIRS * (m % Q):PAIRS * (m % Q + 1), :],
                                     ps_2[m % 2][:, 0:QT].rearrange("p (u s) -> p u s", s=S),
                                     ACT.Relu, bias=b2_sb[:, :]).then_inc(relu2_done, 1)

            def copy_keys(it, sl):
                wait(act, t_done, it, RING * NT, NT * sl + ACT_T + 1)
                copy_bank(lambda out, x: nc.scalar.activation(out, x, ACT.Copy), sl, ACT_T).then_inc(act_copied, 1)

            def copy_scores(it, gl):
                wait(act, l3_done, it, RING, GC * (gl + 1))
                wait(act, exp_done, it, GI, gl - 1)
                nc.scalar.activation(sc[:, gl % 2, :].rearrange("p (r j) -> p r j", j=J),
                                     ps_s[:, 0:S].rearrange("p (j r) -> p r j", r=R),
                                     ACT.Identity, bias=b3_sb[:, :]).then_inc(scores_copied, 1)

            def exps(it, gl):
                par = gl % 2
                wait(act, max_ready, it, GI, gl + 1)
                wait(act, spread[par], it, GI // 2 * 16 * GC, (gl // 2) * 16 * GC)
                nc.scalar.activation(pr[:, par, :], sc[:, par, :], ACT.Exp, bias=nmax[:, par:par + 1],
                                     accum_out=rsum[:, par:par + 1]).then_inc(exp_done, 1)

            def copy_half(it, gl):
                wait(act, out_done, it, GI, gl + 1)
                wait(act, out_ready, it, GI, gl)
                nc.scalar.activation(oh[0:32 + CB, :], ps_o[64:96 + CB, 0:D], ACT.Copy).then_inc(half_copied, 1)

            def body(it, sl):
                for half in range(2):
                    m = Q * (sl - 1) + 2 * half
                    fresh = real(it, sl - 1, NCH, RING)
                    before = real(it, m - 2, NCH * Q, RING * Q)
                    softmax = sl % GC == 1 and half == 1 and real(it, (sl - 3) // GC, NG, GI)
                    if fresh:
                        relu1(it, m)
                        relu1(it, m + 1)
                    if sl % GC == 1 and half == 1 and real(it, (sl - 7) // GC, NG, GI):
                        copy_half(it, (sl - 7) // GC)
                    if fresh:
                        high_part(it, m)
                    if softmax:
                        copy_scores(it, (sl - 3) // GC)
                    if before:
                        relu2(it, m - 2)
                        relu2(it, m - 1)
                    if fresh:
                        high_part(it, m + 1)
                    if half == 0 and real(it, sl, NCH, RING):
                        copy_keys(it, sl)
                    if softmax:
                        exps(it, (sl - 3) // GC)

            steps(act, body)

        @block.tensor
        def _(pe):
            pe.wait_ge(ident_ready, 1)
            pe.wait_ge(query_loaded, 32)
            for n in range(B // P // 4):
                if n >= 2:
                    pe.wait_ge(q_copied, n - 1)
                for t in range(4):
                    mm = pe.transpose(ps_t[n % 2][:, t * P:(t + 1) * P], q_nat[:, 4 * n + t, :], ident[:, :])
                mm.then_inc(q_transposed, 1)
            pe.wait_ge(w1_ready, 2)
            pe.wait_ge(q_copied, B // P // 4)
            for n in range(B // 2 // 512):
                for half in range(2):
                    mm = pe.matmul(ps_1[n % 2][half * H:(half + 1) * H, :], w_query[:, :],
                                   qt[:, 1024 * n + half:1024 * (n + 1):2], start=True, stop=True)
                mm.then_inc(qw_done, 1)
            pe.wait_ge(bias1_ready, B // 2 // 512)
            pe.wait_ge(weights_loaded, 16 * 9)
            pe.wait_ge(consts, 3)


            def transposes(it, sl, t):
                n = NT * sl + t
                if t == 0:
                    pe.wait_ge(keys_loaded[sl], (it + 1) * 16)
                if t - 2 == ACT_T:
                    wait(pe, act_copied, it, RING, sl + 1)
                else:
                    wait(pe, kt_copied, it, RING * (NT - 1), copies(sl, t - 2) + 1)
                for a in range(TSPLIT[t]):
                    j = TSTART[t] + a
                    mm = pe.transpose(ps_t[n % 2][:, a * P:(a + 1) * P], ring[:, sl, j * D:(j + 1) * D], ident[:, :])
                mm.then_inc(t_done, 1)

            def layer1(it, m):
                off = m // Q
                if m % Q == 0:
                    wait(pe, kt_copied, it, RING * (NT - 1), (NT - 1) * (off + 1))
                    wait(pe, act_copied, it, RING, off + 1)
                    wait(pe, we_ready, it, RING, off + 1)
                wait(pe, relu1_done, it, RING * Q, m)
                for n in (m, m + 1):
                    for u in range(PAIRS):
                        for half in range(2):
                            i = QR * (n % Q) + 2 * u + half
                            mm = pe.matmul(ps_1[n % 2][half * H:(half + 1) * H, u * S:(u + 1) * S],
                                           we[:, off % 2, i, :], kt[:, off % 2, :, R * i:R * (i + 1)],
                                           start=True, stop=True)
                    mm.then_inc(l1_done, 1)

            def layer2(it, m, between):
                wait(pe, lo_done, it, RING * Q, m + 2)
                for k in (m, m + 1):
                    bank, n = ps_2[k % 2][:, 0:QT], k % Q
                    pe.matmul(bank, w2_hi[:, :], h1_hi[:, n, :], start=True, stop=False)
                    pe.matmul(bank, w2_hi[:, :], h1_lo[:, n, :], start=False, stop=False)
                    pe.matmul(bank, w2_lo[:, :], h1_hi[:, n, :], start=False, stop=True).then_inc(l2_done, 1)
                    if k == m:
                        between()

            def layer3(it, off):
                wait(pe, relu2_done, it, RING * Q, Q * (off + 1))
                c = off % GC
                if c == 0:
                    wait(pe, scores_copied, it, GI, off // GC)
                for u in range(PAIRS):
                    for q in range(Q):
                        mm = pe.matmul(ps_s[32 * q:32 * q + 32, 0:S], w3_sb[:, PAIRS * c + u, :],
                                       h2[:, off % 2, PAIRS * q + u, :],
                                       start=(c == 0 and u == 0), stop=(c == GC - 1 and u == PAIRS - 1))
                mm.then_inc(l3_done, 1)

            def weighted_sum(it, gl, js):
                par = gl % 2
                if js[0] == 0:
                    wait(pe, pw_ready, it, GI, gl + 1)
                    wait(pe, out_ready, it, GI, gl)
                for j in js:
                    for c in range(GC):
                        p0 = 64 * (j % 2) + 32 * c
                        slot = (GC * gl + c) % RING
                        mm = pe.matmul(ps_o[p0:p0 + CB, 0:D], pw[:, par, c, j, :],
                                       ring[:, slot, j * D:(j + 1) * D], start=(j < 2), stop=(j % 2 == 1 and j + 2 >= PE_SLOTS))
                if js[-1] == PE_SLOTS - 1:
                    mm.then_inc(slots_summed, 1)

            def add_partitions(it, gl):
                par = gl % 2
                wait(pe, dve_added, it, GI * GC * DVE_SLOTS, (gl + 1) * GC * DVE_SLOTS)
                for c in range(GC):
                    mm = pe.matmul(ps_o[32 * c:32 * c + CB, 0:D], own[:, :], part_sum[:, par, c, :],
                                   start=False, stop=True)
                mm.then_inc(out_done, 1)

            def body(it, sl):
                for half in range(2):
                    m = Q * (sl - 1) + 2 * half
                    tiles = [0, 1, 2, 3] if half == 0 else [4, 5, 6]

                    def transpose_next():
                        if tiles and real(it, sl, NCH, RING):
                            transposes(it, sl, tiles.pop(0))

                    if half == 0:
                        transpose_next()
                    if real(it, sl - 1, NCH, RING):
                        layer1(it, m)
                    if half == 1:
                        transpose_next()
                    if half == 1 and real(it, sl - 2, NCH, RING):
                        layer3(it, sl - 2)
                    transpose_next()
                    if real(it, m - 2, NCH * Q, RING * Q):
                        layer2(it, m - 2, transpose_next)
                    else:
                        transpose_next()
                    if half == 0 and sl % GC == 1 and real(it, (sl - 7) // GC, NG, GI):
                        add_partitions(it, (sl - 7) // GC)
                    for (step, h, js) in PE_SUMS:
                        if half == h and sl % GC == step % GC and real(it, (sl - step) // GC, NG, GI):
                            weighted_sum(it, (sl - step) // GC, js)
                    transpose_next()

            steps(pe, body)

        @block.vector
        def _(dve):
            nc.vector.memset(w2_sb[:, :], 0.0).then_inc(w2_cleared, 1)
            nc.vector.memset(w3_sb[:, :, :], 0.0).then_inc(w1_ready, 1)
            nc.vector.memset(neg[:, :], NEG_INF)
            nc.vector.memset(ps_o[:, :], 0.0)
            nc.vector.memset(ring[:, RING - 4:RING - 2, :].rearrange("p a f -> p (a f)"), 0.0).then_inc(stage_cleared_dve, 1)
            dve.wait_ge(query_loaded, 32)
            nc.vector.tensor_tensor(w_query[:, :], w1_sb[:, 0, :], w1_sb[:, 2, :], ALU.add)
            nc.vector.tensor_tensor(w_key[:, :], w1_sb[:, 1, :], w1_sb[:, 2, :], ALU.subtract).then_inc(w1_ready, 1)
            for n in range(B // P // 4):
                dve.wait_ge(q_transposed, n + 1)
                nc.vector.tensor_copy(qt[:, 512 * n:512 * (n + 1)], ps_t[n % 2][:, :]).then_inc(q_copied, 1)
            dve.wait_ge(weights_loaded, 16 * 9)
            dve.wait_ge(w1_ready, 1)
            for c in range(GC):
                for u in range(PAIRS):
                    for half in range(2):
                        col = R * (2 * u + half) + c
                        ins = nc.vector.tensor_copy(w3_sb[half * H:(half + 1) * H, PAIRS * c + u, col:col + 1],
                                                    w3_col[half * H:(half + 1) * H, :])
            ins.then_inc(consts, 1)
            nc.vector.tensor_copy(w2_hi[:, :], w2_sb[:, :]).then_inc(consts, 1)
            dve.wait_ge(consts, 2)
            nc.vector.tensor_tensor(w2_lo[:, :], w2_sb[:, :], w2_hi[:, :].bitcast(F32), ALU.subtract).then_inc(consts, 1)

            def convert_mask(n):
                part = slice(n * NG // CONV, (n + 1) * NG // CONV)
                dve.wait_ge(mask_loaded, 16 * 2 * GC)
                nc.vector.tensor_scalar(dropped[:, part, :], mstage[:, part, :], 0, None, ALU.is_equal).then_inc(mask_done, 1)

            def copy_keys(it, sl, t):
                n = NT * sl + t
                wait(dve, t_done, it, RING * NT, n + 1)
                if t == 0:
                    wait(dve, l1_done, it, RING * Q, Q * (sl - 1))
                copy_bank(nc.vector.tensor_copy, sl, t).then_inc(kt_copied, 1)

            def low_part(it, m):
                wait(dve, hi_done, it, RING * Q, m + 1)
                nc.vector.tensor_tensor(h1_lo[:, m % Q, :], h1[:, m % 2, :], h1_hi[:, m % Q, :].bitcast(F32),
                                        ALU.subtract).then_inc(lo_done, 1)

            def mask_and_max(it, gl):
                par = gl % 2
                nc.vector.copy_predicated(sc[:, par, :], drop[:, par, :], neg[:, :]).then_inc(masked, 1)
                wait(dve, masked, it, GI, gl + 1)
                nc.vector.tensor_reduce(nmax[:, par:par + 1], sc[:, par, :], AX.X, ALU.max, negate=True).then_inc(max_ready, 1)

            def normalize(it, gl):
                par = gl % 2
                wait(dve, exp_done, it, GI, gl + 1)
                nc.vector.reciprocal(rinv[:, par:par + 1], rsum[:, par:par + 1]).then_inc(rinv_ready, 1)
                wait(dve, rinv_ready, it, GI, gl + 1)
                nc.vector.tensor_scalar(pr[:, par, :], pr[:, par, :], rinv[:, par:par + 1], None,
                                        ALU.mult).then_inc(probs_ready, 1)

            def add_halves(it, gl):
                par = gl % 2
                wait(dve, half_copied, it, GI, gl + 1)
                wait(dve, stored[par], it, GI // 2 * 16 * GC, (gl // 2) * 16 * GC)
                nc.vector.tensor_tensor(osb[0:32 + CB, par, :], ps_o[0:32 + CB, 0:D], oh[0:32 + CB, :],
                                        ALU.add).then_inc(out_ready, 1)

            def add_slot(it, gl, n):
                par, j = gl % 2, J - DVE_SLOTS + n
                if n == 0:
                    wait(dve, pool_added, it, GI, gl + 1)
                for c in range(GC):
                    if n > 0:
                        wait(dve, dve_added, it, GI * GC * DVE_SLOTS, GC * (gl * DVE_SLOTS + n - 1) + c + 1)
                    nc.vector.scalar_tensor_tensor(
                        out=part_sum[:, par, c, :], in0=ring[:, (GC * gl + c) % RING, j * D:(j + 1) * D],
                        scalar=pn[:, par, c, j:j + 1], in1=part_sum[:, par, c, :],
                        op0=ALU.mult, op1=ALU.add).then_inc(dve_added, 1)

            def body(it, sl):
                for t in range(NT):
                    new = real(it, sl, NCH, RING)
                    m = Q * (sl - 1) + (0 if t < 4 else 2)
                    softmax = sl % GC == 1 and real(it, (sl - 3) // GC, NG, GI)
                    if t == 6 and softmax:
                        wait(dve, scores_copied, it, GI, (sl - 3) // GC + 1)
                        wait(dve, drop_ready, it, GI, (sl - 3) // GC + 1)
                    if new and t != ACT_T:
                        copy_keys(it, sl, t)
                    if t == 6 and softmax:
                        mask_and_max(it, (sl - 3) // GC)
                    if t in (1, 2, 5, 6) and real(it, sl - 1, NCH, RING):
                        low_part(it, m + (t in (2, 6)))
                    if t == 0 and sl % GC == 0 and real(it, (sl - 4) // GC, NG, GI):
                        normalize(it, (sl - 4) // GC)
                    if t == 6 and sl % GC == 1 and real(it, (sl - 7) // GC, NG, GI):
                        add_halves(it, (sl - 7) // GC)
                    for n, (step, place) in enumerate(DVE_SUMS):
                        if t == place and sl % GC == step % GC and real(it, (sl - step) // GC, NG, GI):
                            add_slot(it, (sl - step) // GC, n)
                    if isinstance(it, int) and it == 0 and sl == 2:
                        convert_mask(t)

            steps(dve, body)


_INS = ["r_query", "r_keys", "r_mask", "L0_rec_W1", "L0_rec_b1", "L0_rec_W2", "L0_rec_b2", "L0_rec_W3", "L0_rec_b3"]


def kernel(**inputs):
    import numpy as _np
    import concourse.bacc as _bacc
    from concourse import mybir as _mybir
    from concourse.bass_utils import run_bass_kernel_spmd as _run

    nc = _bacc.Bacc("TRN2", target_bir_lowering=False, num_devices=1)
    arrays, args = {}, []
    for name in _INS:
        a = _np.ascontiguousarray(inputs[name])
        arrays[f"in_{name}"] = a
        args.append(nc.dram_tensor(f"in_{name}", a.shape, _mybir.dt.from_np(a.dtype), kind="ExternalInput").ap())
    b, _, d = inputs["r_keys"].shape
    out = nc.dram_tensor("out_0", (b, d), _mybir.dt.float32, kind="ExternalOutput").ap()
    din_attention(nc, *args, out)
    r = _run(nc, [arrays], core_ids=[0])
    return r.results[0]["out_0"]
```
